# Optimizing a Trainium2 kernel written in Bass

```python
import numpy as np
import jax
import jax.numpy as jnp

def _softmax(x, axis=-1):
    return jax.nn.softmax(x, axis=axis)

def _gelu(x):
    return jax.nn.gelu(x, approximate=True)

def _silu(x):
    return jax.nn.silu(x)

def _sigmoid(x):
    return jax.nn.sigmoid(x)

def _layernorm(x, axis=-1, eps=1e-05):
    m = jnp.mean(x, axis=axis, keepdims=True)
    v = jnp.var(x, axis=axis, keepdims=True)
    return (x - m) / jnp.sqrt(v + eps)

def _scatter_add(tgt, idx, src, axis=0):
    return tgt.at[idx].add(src)

def _segment_sum(src, seg, n):
    return jax.ops.segment_sum(src, seg, n)
kernel_name = 'mk_gps_d1_gnn_r8_a14c37'

def setup_inputs(seed: int=0):
    np.random.seed(seed)
    _w = jnp.asarray

    def _rec_inputs():
        import jax
        import jax.numpy as jnp
        _gk = jax.random.key(seed)
        x = -0.000364 + 1 * jax.random.normal(jax.random.fold_in(_gk, 1), (1250, 768), jnp.float32)
        src = jax.random.randint(jax.random.fold_in(_gk, 2), (40000,), 0, 1250, jnp.int32)
        dst = jnp.minimum((1250 * jax.random.uniform(jax.random.fold_in(_gk, 3), (40000,)) ** 2.0).astype(jnp.int32), 9999)
        _o = jnp.argsort(dst, stable=True)
        src = src[_o]
        dst = dst[_o]
        return (x, src, dst)
    x, src, dst = _rec_inputs()

    def _L0_gnn_setup():
        import jax, jax.numpy as jnp
        import numpy as np
        N_NODES = 2500
        N_EDGES = 20000
        IN_DIM = 768
        HID = 256
        HEADS = 4
        OUT_DIM = 768
        LN_EPS = 1e-05

        def _add_self_loops(edge_index, n):
            loop = jnp.arange(n, dtype=edge_index.dtype)
            return jnp.concatenate([edge_index, jnp.stack([loop, loop])], axis=1)

        def gat_conv(x, edge_index, W, a_src, a_dst, bias, heads, out_ch, concat):
            n = x.shape[0]
            ei = _add_self_loops(edge_index, n)
            src, dst = (ei[0], ei[1])
            xl = (x @ W).reshape(n, heads, out_ch)
            alpha_src = jnp.einsum('nhc,hc->nh', xl, a_src)
            alpha_dst = jnp.einsum('nhc,hc->nh', xl, a_dst)
            e = jax.nn.leaky_relu(alpha_src[src] + alpha_dst[dst], 0.2)
            m = jax.ops.segment_max(e, dst, num_segments=n)
            e = jnp.exp(e - m[dst])
            s = jax.ops.segment_sum(e, dst, num_segments=n)
            alpha = e / (s[dst] + 1e-16)
            msg = xl[src] * alpha[:, :, None]
            out = jax.ops.segment_sum(msg, dst, num_segments=n)
            out = out.reshape(n, heads * out_ch) if concat else out.mean(axis=1)
            return out + bias

        def layer_norm(x, g, b):
            mu = jnp.mean(x, axis=-1, keepdims=True)
            var = jnp.var(x, axis=-1, keepdims=True)
            return (x - mu) * jax.lax.rsqrt(var + LN_EPS) * g + b
        key = jax.random.key(seed)
        ks = jax.random.split(key, 16)
        s = 0.02
        HC = HID * HEADS
        return {'x': jax.random.normal(ks[0], (N_NODES, IN_DIM), jnp.float32), 'edge_index': jax.random.randint(ks[1], (2, N_EDGES), 0, N_NODES, jnp.int64 if jax.config.jax_enable_x64 else jnp.int32), 'W1': jax.random.normal(ks[2], (IN_DIM, HC), jnp.float32) * s, 'a_src1': jax.random.normal(ks[3], (HEADS, HID), jnp.float32) * s, 'a_dst1': jax.random.normal(ks[4], (HEADS, HID), jnp.float32) * s, 'b1': jnp.zeros((HC,), jnp.float32), 'g1': jnp.ones((HC,), jnp.float32), 'be1': jnp.zeros((HC,), jnp.float32), 'Wr1': jax.random.normal(ks[5], (IN_DIM, HC), jnp.float32) * s, 'br1': jnp.zeros((HC,), jnp.float32), 'W2': jax.random.normal(ks[6], (HC, OUT_DIM), jnp.float32) * s, 'a_src2': jax.random.normal(ks[7], (1, OUT_DIM), jnp.float32) * s, 'a_dst2': jax.random.normal(ks[8], (1, OUT_DIM), jnp.float32) * s, 'b2': jnp.zeros((OUT_DIM,), jnp.float32), 'g2': jnp.ones((OUT_DIM,), jnp.float32), 'be2': jnp.zeros((OUT_DIM,), jnp.float32), 'Wr2': jax.random.normal(ks[9], (HC, OUT_DIM), jnp.float32) * s, 'br2': jnp.zeros((OUT_DIM,), jnp.float32)}
    _L0_gnn_all = _L0_gnn_setup()
    _L0_gnn_in = {k: v for k, v in _L0_gnn_all.items() if k in ('W1', 'a_src1', 'a_dst1', 'b1', 'g1', 'be1', 'Wr1', 'br1', 'W2', 'a_src2', 'a_dst2', 'b2', 'g2', 'be2', 'Wr2', 'br2')}
    del _L0_gnn_all

    def _L0_mix_setup():
        import jax, jax.numpy as jnp
        import numpy as np
        H = 12
        D = 64
        EPS = 1e-06

        def _phi(x):
            return jnp.where(x > 0, x + 1.0, jnp.exp(x))
        key = jax.random.key(seed)
        k1, k2, k3 = jax.random.split(key, 3)
        B, N, C = (4, 1024, 768)
        x = jax.random.normal(k1, (B, N, C), dtype=jnp.float32)
        W_qkv = jax.random.normal(k2, (C, 3 * C), dtype=jnp.float32) * C ** (-0.5)
        b_qkv = jnp.zeros((3 * C,), dtype=jnp.float32)
        W_out = jax.random.normal(k3, (C, C), dtype=jnp.float32) * C ** (-0.5)
        b_out = jnp.zeros((C,), dtype=jnp.float32)
        return {'x': x, 'W_qkv': W_qkv, 'b_qkv': b_qkv, 'W_out': W_out, 'b_out': b_out}
    _L0_mix_all = _L0_mix_setup()
    _L0_mix_in = {k: v for k, v in _L0_mix_all.items() if k in ('W_qkv', 'b_qkv', 'W_out', 'b_out')}
    del _L0_mix_all

    def _L0_ffn_setup():
        import jax, jax.numpy as jnp
        import numpy as np
        B, N, C, H, E = (8, 1024, 768, 384, 4)
        key = jax.random.key(seed)
        ks = jax.random.split(key, 8)
        s_in = 1.0 / np.sqrt(C)
        s_h = 1.0 / np.sqrt(H)
        return {'x': jax.random.normal(ks[0], (B, N, C), dtype=jnp.float32), 'gate_w': jax.random.normal(ks[1], (C, E), dtype=jnp.float32) * 0.01, 'gate_b': jnp.zeros((E,), dtype=jnp.float32), 'gate_center': jnp.zeros((E,), dtype=jnp.float32), 'w1': jax.random.uniform(ks[2], (E, C, H), jnp.float32, -s_in, s_in), 'b1': jax.random.uniform(ks[3], (E, H), jnp.float32, -s_in, s_in), 'w2': jax.random.uniform(ks[4], (E, H, C), jnp.float32, -s_h, s_h), 'b2': jax.random.uniform(ks[5], (E, C), jnp.float32, -s_h, s_h)}
    _L0_ffn_all = _L0_ffn_setup()
    _L0_ffn_in = {k: v for k, v in _L0_ffn_all.items() if k in ('gate_w', 'gate_b', 'gate_center', 'w1', 'b1', 'w2', 'b2')}
    del _L0_ffn_all
    return {'x': x, 'src': src, 'dst': dst, 'L0_gnn_W1': _L0_gnn_in['W1'], 'L0_gnn_a_src1': _L0_gnn_in['a_src1'], 'L0_gnn_a_dst1': _L0_gnn_in['a_dst1'], 'L0_gnn_b1': _L0_gnn_in['b1'], 'L0_gnn_g1': _L0_gnn_in['g1'], 'L0_gnn_be1': _L0_gnn_in['be1'], 'L0_gnn_Wr1': _L0_gnn_in['Wr1'], 'L0_gnn_br1': _L0_gnn_in['br1'], 'L0_gnn_W2': _L0_gnn_in['W2'], 'L0_gnn_a_src2': _L0_gnn_in['a_src2'], 'L0_gnn_a_dst2': _L0_gnn_in['a_dst2'], 'L0_gnn_b2': _L0_gnn_in['b2'], 'L0_gnn_g2': _L0_gnn_in['g2'], 'L0_gnn_be2': _L0_gnn_in['be2'], 'L0_gnn_Wr2': _L0_gnn_in['Wr2'], 'L0_gnn_br2': _L0_gnn_in['br2'], 'L0_mix_W_qkv': _L0_mix_in['W_qkv'], 'L0_mix_b_qkv': _L0_mix_in['b_qkv'], 'L0_mix_W_out': _L0_mix_in['W_out'], 'L0_mix_b_out': _L0_mix_in['b_out'], 'L0_ffn_gate_w': _L0_ffn_in['gate_w'], 'L0_ffn_gate_b': _L0_ffn_in['gate_b'], 'L0_ffn_gate_center': _L0_ffn_in['gate_center'], 'L0_ffn_w1': _L0_ffn_in['w1'], 'L0_ffn_b1': _L0_ffn_in['b1'], 'L0_ffn_w2': _L0_ffn_in['w2'], 'L0_ffn_b2': _L0_ffn_in['b2']}

def reference(x, src, dst, L0_gnn_W1, L0_gnn_a_src1, L0_gnn_a_dst1, L0_gnn_b1, L0_gnn_g1, L0_gnn_be1, L0_gnn_Wr1, L0_gnn_br1, L0_gnn_W2, L0_gnn_a_src2, L0_gnn_a_dst2, L0_gnn_b2, L0_gnn_g2, L0_gnn_be2, L0_gnn_Wr2, L0_gnn_br2, L0_mix_W_qkv, L0_mix_b_qkv, L0_mix_W_out, L0_mix_b_out, L0_ffn_gate_w, L0_ffn_gate_b, L0_ffn_gate_center, L0_ffn_w1, L0_ffn_b1, L0_ffn_w2, L0_ffn_b2):
    import jax
    import jax.numpy as jnp

    def _L0_gnn_ref(x, edge_index, W1, a_src1, a_dst1, b1, g1, be1, Wr1, br1, W2, a_src2, a_dst2, b2, g2, be2, Wr2, br2):
        import jax, jax.numpy as jnp
        import numpy as np
        N_NODES = 2500
        N_EDGES = 20000
        IN_DIM = 768
        HID = 256
        HEADS = 4
        OUT_DIM = 768
        LN_EPS = 1e-05

        def _add_self_loops(edge_index, n):
            loop = jnp.arange(n, dtype=edge_index.dtype)
            return jnp.concatenate([edge_index, jnp.stack([loop, loop])], axis=1)

        def gat_conv(x, edge_index, W, a_src, a_dst, bias, heads, out_ch, concat):
            n = x.shape[0]
            ei = _add_self_loops(edge_index, n)
            src, dst = (ei[0], ei[1])
            xl = (x @ W).reshape(n, heads, out_ch)
            alpha_src = jnp.einsum('nhc,hc->nh', xl, a_src)
            alpha_dst = jnp.einsum('nhc,hc->nh', xl, a_dst)
            e = jax.nn.leaky_relu(alpha_src[src] + alpha_dst[dst], 0.2)
            m = jax.ops.segment_max(e, dst, num_segments=n)
            e = jnp.exp(e - m[dst])
            s = jax.ops.segment_sum(e, dst, num_segments=n)
            alpha = e / (s[dst] + 1e-16)
            msg = xl[src] * alpha[:, :, None]
            out = jax.ops.segment_sum(msg, dst, num_segments=n)
            out = out.reshape(n, heads * out_ch) if concat else out.mean(axis=1)
            return out + bias

        def layer_norm(x, g, b):
            mu = jnp.mean(x, axis=-1, keepdims=True)
            var = jnp.var(x, axis=-1, keepdims=True)
            return (x - mu) * jax.lax.rsqrt(var + LN_EPS) * g + b
        h0 = x
        h = gat_conv(x, edge_index, W1, a_src1, a_dst1, b1, HEADS, HID, True)
        h = layer_norm(h, g1, be1)
        h = jax.nn.relu(h)
        h = h + (h0 @ Wr1 + br1)
        h1 = h
        h = gat_conv(h, edge_index, W2, a_src2, a_dst2, b2, 1, OUT_DIM, False)
        h = layer_norm(h, g2, be2)
        h = h + (h1 @ Wr2 + br2)
        return h

    def _L0_mix_ref(x, W_qkv, b_qkv, W_out, b_out):
        import jax, jax.numpy as jnp
        import numpy as np
        H = 12
        D = 64
        EPS = 1e-06

        def _phi(x):
            return jnp.where(x > 0, x + 1.0, jnp.exp(x))
        B, N, C = x.shape
        qkv = x @ W_qkv + b_qkv
        qkv = qkv.reshape(B, N, 3, H, D).transpose(2, 0, 3, 1, 4)
        q, k, v = (qkv[0], qkv[1], qkv[2])
        qf = _phi(q)
        kf = _phi(k)
        kv = jnp.einsum('bhnd,bhne->bhde', kf.astype(jnp.float32), v.astype(jnp.float32)).astype(v.dtype)
        y_num = jnp.einsum('bhnd,bhde->bhne', qf, kv)
        z = kf.astype(jnp.float32).sum(axis=2)
        y_den = jnp.einsum('bhnd,bhd->bhn', qf, z.astype(qf.dtype))
        y_den = jnp.maximum(y_den[..., None], EPS)
        y = (y_num / y_den).transpose(0, 2, 1, 3).reshape(B, N, C)
        return y @ W_out + b_out

    def _L0_ffn_ref(x, gate_w, gate_b, gate_center, w1, b1, w2, b2):
        import jax, jax.numpy as jnp
        import numpy as np
        B, N, C, H, E = (8, 1024, 768, 384, 4)
        b, n, c = x.shape
        scores = jnp.einsum('bnc,ce->bne', x, gate_w) + gate_b
        p_experts = jax.nn.softmax(scores - gate_center, axis=-1)
        expert = jnp.argmax(p_experts, axis=-1).reshape(-1)
        xt = x.reshape(-1, c)
        h = jax.nn.gelu(jnp.einsum('tc,ech->eth', xt, w1) + b1[:, None, :], approximate=False)
        out_all = jnp.einsum('eth,ehc->etc', h, w2) + b2[:, None, :]
        out = jnp.take_along_axis(out_all, expert[None, :, None], axis=0)[0]
        return out.reshape(b, n, c)
    edge_index = jnp.stack([src, dst])
    xn = _layernorm(x, axis=-1)
    x = x + _L0_gnn_ref(xn, edge_index, L0_gnn_W1, L0_gnn_a_src1, L0_gnn_a_dst1, L0_gnn_b1, L0_gnn_g1, L0_gnn_be1, L0_gnn_Wr1, L0_gnn_br1, L0_gnn_W2, L0_gnn_a_src2, L0_gnn_a_dst2, L0_gnn_b2, L0_gnn_g2, L0_gnn_be2, L0_gnn_Wr2, L0_gnn_br2) + _L0_mix_ref(xn[None], L0_mix_W_qkv, L0_mix_b_qkv, L0_mix_W_out, L0_mix_b_out)[0]
    x = x + _L0_ffn_ref(_layernorm(x, axis=-1)[None], L0_ffn_gate_w, L0_ffn_gate_b, L0_ffn_gate_center, L0_ffn_w1, L0_ffn_b1, L0_ffn_w2, L0_ffn_b2)[0]
    return x

_drawn_inputs = setup_inputs


def setup_inputs(seed=0):
    import zlib

    import numpy as np

    out = dict(_drawn_inputs(seed))
    spreads = {'L0_gnn_b1': (0.0, 0.1),
     'L0_gnn_g1': (1.0, 0.2),
     'L0_gnn_be1': (0.0, 0.1),
     'L0_gnn_br1': (0.0, 0.1),
     'L0_gnn_b2': (0.0, 0.1),
     'L0_gnn_g2': (1.0, 0.2),
     'L0_gnn_be2': (0.0, 0.1),
     'L0_gnn_br2': (0.0, 0.1),
     'L0_mix_b_qkv': (0.0, 0.1),
     'L0_mix_b_out': (0.0, 0.1),
     'L0_ffn_gate_b': (0.0, 0.1),
     'L0_ffn_gate_center': (0.0, 0.1)}
    factors = {'L0_gnn_a_dst1': 28.59, 'L0_gnn_a_dst2': 9.233, 'L0_ffn_b1': 8.0, 'L0_ffn_b2': 3.103}
    for name, (base, spread) in spreads.items():
        noise = np.random.default_rng([zlib.crc32(name.encode()), seed]).standard_normal(out[name].shape)
        drawn = base * np.exp(spread * noise) if base else spread * noise
        out[name] = jnp.asarray(drawn.astype(out[name].dtype))
    for name, factor in factors.items():
        out[name] = (out[name] * factor).astype(out[name].dtype)
    return out
```

```python
from contextlib import ExitStack

import concourse.bass as bass
from concourse import mybir

F32 = mybir.dt.float32
BF16 = mybir.dt.bfloat16
U16 = mybir.dt.uint16
I32 = mybir.dt.int32
ALU = mybir.AluOpType
ACT = mybir.ActivationFunctionType
AX_X = mybir.AxisListType.X

NEG = -1.0e30
KB = 256

N, D = 1250, 768
R = 125
T = N // R
KD = D // 128
HEADS, HID = 4, 256
HC = HEADS * HID
KH = HC // 128
EDGES = 40000
CH = 125
QC = 4
QUADS = EDGES // (CH * QC)
E_FFN, H_FFN = 4, 384
KF = H_FFN // 128
SPANS = [(0, 500), (500, 500), (1000, 250)]
GROUPS = [(0, 4), (4, 3), (7, 3)]
LN_EPS = 1e-5
MIX_EPS = 1e-6


class Shared:
    pass


class Chain:

    def __init__(self, eng, s):
        self.eng, self.sem, self.count = eng, s, 0

    def __call__(self, ins):
        self.count += 1
        ins.then_inc(self.sem, 1)
        self.eng.wait_ge(self.sem, self.count)


def area(m, kb, words, parts=128):
    return m.arena[0:parts, int(kb * KB):int(kb * KB) + words]


def rows_of(v, n=R):
    return v.rearrange("(o n) -> o n", o=1).broadcast_to([n, v.shape[0]])


def tile_rows(d, t):
    return d[t * R:(t + 1) * R, :]


def slab_of(w, c, n):
    return w[:, c:c + n].rearrange("(k p) c -> p k c", p=128)


def moments(dve, link, stats, t, src, mv, done):
    half = src.shape[1] // 2
    if t >= 2:
        dve.wait_ge(done, t - 1)
    dve.bn_stats(stats[0:R, t % 2, 0:6], src[:, 0:half]).then_inc(link.sem, 1)
    link.count += 1
    link(dve.bn_stats(stats[0:R, t % 2, 6:12], src[:, half:2 * half]))
    dve.bn_aggr(mv[0:R, t, :], stats[0:R, t % 2, :]).then_inc(done, 1)


def mixer_phase(nc, m, io):
    X = area(m, 0, T * D, R).rearrange("p (t c) -> p t c", t=T)
    QT = area(m, 30, KD * N).rearrange("p (k n) -> p k n", k=KD)
    K = area(m, 60, T * D, R).rearrange("p (t c) -> p t c", t=T)
    V = area(m, 120, T * D, R).rearrange("p (t c) -> p t c", t=T)
    W_SLOT = [area(m, 150 + 9 * i, KD * 384).rearrange("p (k c) -> p k c", k=KD) for i in range(2)]
    XN = [area(m, 168 + 3 * i, D, R) for i in range(2)]
    KVB = area(m, 168, KD * 256).rearrange("p (k a c) -> p k a c", k=KD, a=2)
    BROW = area(m, 174, 2 * D, R)
    BO = area(m, 180, D, R)
    TM = [area(m, 183 + 2 * i, 500) for i in range(2)]
    BD = area(m, 187, 128)
    BQ = area(m, 187.5, KD)
    XNT, ps = m.XNT, m.ps

    x_in, w_in = m.sems("x_in", T), m.sems("w_qkv_in", 2)
    b_in, const_ok = m.sem("b_in"), m.sem("const_ok")
    mv_ok, sd_ok, xn_ok, xt_ok, xnt_ok, xb_ok = (m.sem(s) for s in ("mv_ok", "sd_ok", "xn_ok", "xt_ok", "xnt_ok", "xb_ok"))
    prod_ok, prod_out, min_ok, exp_ok, phi_ok = (m.sem(s) for s in ("prod_ok", "prod_out", "min_ok", "exp_ok", "phi_ok"))
    kv_ok, kvb_ok, y_ok, yt_ok, o_ok, o_out, res_out = (
        m.sem(s) for s in ("kv_ok", "kvb_ok", "y_ok", "yt_ok", "o_ok", "o_out", "res_out"))
    dve_own = m.sem("dve_own1")

    UNITS = ([("q", s, (i, j)) for s in range(2) for i in range(3) for j in range(3)]
             + [("k", s, t) for s in range(2) for t in range(T)] + [("v", s, t) for s in range(2) for t in range(T)])
    NPHI = len(UNITS) - 2 * T
    slab_no = [{"q": 0, "k": 2, "v": 4}[kind] + s for kind, s, _ in UNITS]
    units_to = [sum(1 for x in slab_no if x <= i) for i in range(6)]

    def unit_out(u):
        kind, s, at = UNITS[u]
        if kind == "q":
            c, w = SPANS[at[1]]
            return QT[:, 3 * s + at[0], c:c + w]
        return (K if kind == "k" else V)[:, at, 384 * s:384 * s + 384]

    with nc.Block() as block:
        @block.sync
        def _(sp):
            for t in range(T):
                sp.dma_start(X[:, t, :], tile_rows(io.x, t)).then_inc(x_in[t], 16)
                if t < 2:
                    sp.dma_start(W_SLOT[t], slab_of(io.W_qkv, 384 * t, 384)).then_inc(w_in[t], 16)
            sp.dma_start(BROW, rows_of(io.b_qkv[D:3 * D])).then_inc(b_in, 16)
            sp.dma_start(BO, rows_of(io.b_out)).then_inc(b_in, 16)
            with nc.allow_non_contiguous_dma(reason="768 words, once"):
                sp.dma_start(BQ, io.b_qkv[0:D].rearrange("(k p) -> p k", p=128)).then_inc(b_in, 16)
            for i in range(2, 8):
                sp.wait_ge(prod_ok, units_to[i - 2])
                w = slab_of(io.W_qkv, 384 * i, 384) if i < 6 else slab_of(io.W_out, 384 * (i - 6), 384)
                sp.dma_start(W_SLOT[i % 2], w).then_inc(w_in[i % 2], 16)
            for t in range(T):
                sp.wait_ge(o_out, T + t + 1)
                sp.dma_start(tile_rows(m.res_d, t), X[:, t, :]).then_inc(res_out, 16)
            sp.wait_ge(res_out, 16 * T)

        @block.gpsimd
        def _(pool):
            pool.memset(m.ident[:], 0.0).then_inc(const_ok, 1)
            pool.memset(m.ones[:], 1.0).then_inc(const_ok, 1)
            pool.memset(m.eps[:], LN_EPS).then_inc(const_ok, 1)
            pool.memset(BD, 0.0).then_inc(const_ok, 1)
            pool.wait_ge(const_ok, 4)
            pool.affine_select(out=m.ident[:], in_=m.ident[:], compare_op=ALU.not_equal, fill=1.0, base=0,
                               pattern=[[-1, 128]], channel_multiplier=1).then_inc(const_ok, 1)
            pool.wait_ge(const_ok, 5)
            pool.memset(BD[0:64, 0:64], 1.0).then_inc(const_ok, 1)
            pool.wait_ge(const_ok, 6)
            pool.memset(BD[64:128, 64:128], 1.0).then_inc(const_ok, 1)
            pool.wait_ge(const_ok, 7)
            pool.wait_ge(b_in, 48)
            for t in range(T):
                pool.wait_ge(xn_ok, t + 1)
                pool.tensor_tensor(X[:, t, :], X[:, t, :], BO, ALU.add).then_inc(xb_ok, 1)
            for u in range(NPHI):
                z = unit_out(u)
                pool.wait_ge(prod_out, u + 1)
                if u >= 2:
                    pool.wait_ge(phi_ok, u - 1)
                tm = TM[u % 2][0:z.shape[0], 0:z.shape[1]]
                pool.tensor_scalar(tm, z, 0.0, None, ALU.min).then_inc(min_ok, 1)

        @block.scalar
        def _(act):
            def copy_xt(t):
                for j in range(2):
                    act.wait_ge(xt_ok, 2 * t + j + 1)
                    act.copy(XNT[:, 3 * j:3 * j + 3, R * t:R * t + R],
                             ps[:, 2 * (t % 2) + j, 0:3 * R].rearrange("p (k n) -> p k n", k=3)).then_inc(xnt_ok, 1)

            act.wait_ge(const_ok, 3)
            for t in range(T):
                act.wait_ge(mv_ok, t + 1)
                act.activation(m.sd[0:R, t:t + 1], m.mv[0:R, t, 1:2], ACT.Sqrt, bias=m.eps[0:R, :]).then_inc(sd_ok, 1)
                if t >= 1:
                    copy_xt(t - 1)
            copy_xt(T - 1)
            for u in range(NPHI):
                z = unit_out(u)
                act.wait_ge(min_ok, u + 1)
                tm = TM[u % 2][0:z.shape[0], 0:z.shape[1]]
                act.activation(tm, tm, ACT.Exp).then_inc(exp_ok, 1)

        @block.vector
        def _(dve):
            link = Chain(dve, dve_own)

            def normalise(t):
                dve.wait_ge(sd_ok, t + 1)
                link(dve.reciprocal(m.rstd[0:R, t:t + 1], m.sd[0:R, t:t + 1]))
                if t >= 2:
                    dve.wait_ge(xt_ok, 2 * (t - 1))
                dve.tensor_scalar(XN[t % 2], X[:, t, :], m.mv[0:R, t, 0:1], m.rstd[0:R, t:t + 1],
                                  ALU.subtract, ALU.mult).then_inc(xn_ok, 1)

            for t in range(T):
                dve.wait_ge(x_in[t], 16)
                moments(dve, link, m.stats, t, X[:, t, :], m.mv, mv_ok)
                if t >= 1:
                    normalise(t - 1)
            normalise(T - 1)
            dve.wait_ge(b_in, 48)

            def finish_phi(u):
                z = unit_out(u)
                dve.wait_ge(exp_ok, u + 1)
                tm = TM[u % 2][0:z.shape[0], 0:z.shape[1]]
                dve.scalar_tensor_tensor(out=z, in0=z, scalar=0.0, in1=tm, op0=ALU.max, op1=ALU.add).then_inc(phi_ok, 1)

            for u, (kind, s, at) in enumerate(UNITS):
                z = unit_out(u)
                p, w = z.shape
                dve.wait_ge(prod_ok, u + 1)
                if kind == "q":
                    dve.tensor_scalar(z, ps[0:p, u % 4, 0:w], BQ[:, 3 * s + at[0]:3 * s + at[0] + 1], None,
                                      ALU.add).then_inc(prod_out, 1)
                else:
                    c = (0 if kind == "k" else D) + 384 * s
                    dve.tensor_tensor(z, ps[0:p, u % 4, 0:w], BROW[:, c:c + w], ALU.add).then_inc(prod_out, 1)
                if 2 <= u < NPHI + 2:
                    finish_phi(u - 2)
            for j in range(KD):
                dve.wait_ge(kv_ok, j + 1)
                dve.tensor_tensor(KVB[:, j, :, :], ps[:, 4 + j % 2, 0:256].rearrange("p (a c) -> p a c", a=2),
                                  BD.unsqueeze(1).broadcast_to([128, 2, 128]), ALU.mult).then_inc(kvb_ok, 1)
            dve.wait_ge(phi_ok, NPHI)
            for u in range(3 * KD):
                j, (c, w), b = u // 3, SPANS[u % 3], 2 * (u % 2)
                dve.wait_ge(y_ok, u + 1)
                link(dve.tensor_scalar(TM[0][:, 0:w], ps[:, b + 1, 0:w], MIX_EPS, None, ALU.max))
                link(dve.reciprocal(TM[1][:, 0:w], TM[0][:, 0:w]))
                dve.tensor_tensor(QT[:, j, c:c + w], ps[:, b, 0:w], TM[1][:, 0:w], ALU.mult).then_inc(yt_ok, 1)
            dve.wait_ge(xb_ok, T)
            for u in range(2 * T):
                s, t = divmod(u, T)
                dve.wait_ge(o_ok, u + 1)
                part = X[:, t, 384 * s:384 * s + 384]
                dve.tensor_tensor(part, ps[0:R, 4 + u % 4, 0:384], part, ALU.add).then_inc(o_out, 1)

        @block.tensor
        def _(pe):
            pe.wait_ge(const_ok, 7)
            for t in range(T):
                pe.wait_ge(xn_ok, t + 1)
                for j in range(2):
                    if t >= 2:
                        pe.wait_ge(xnt_ok, 2 * (t - 2) + j + 1)
                    for k in range(3):
                        tr = pe.transpose(ps[:, 2 * (t % 2) + j, R * k:R * k + R],
                                          XN[t % 2][:, (3 * j + k) * 128:(3 * j + k + 1) * 128], m.ident[0:R, 0:R])
                    tr.then_inc(xt_ok, 1)
            pe.wait_ge(xnt_ok, 2 * T)
            for u, (kind, s, at) in enumerate(UNITS):
                slab = slab_no[u]
                pe.wait_ge(w_in[slab % 2], 16 * (slab // 2 + 1))
                if u >= 4:
                    pe.wait_ge(prod_out, u - 3)
                p, w = unit_out(u).shape
                for k in range(KD):
                    if kind == "q":
                        c, _ = SPANS[at[1]]
                        a, b = W_SLOT[slab % 2][:, k, 128 * at[0]:128 * at[0] + 128], XNT[:, k, c:c + w]
                    else:
                        a, b = XNT[:, k, R * at:R * at + R], W_SLOT[slab % 2][:, k, :]
                    mm = pe.matmul(ps[0:p, u % 4, 0:w], a, b, start=k == 0, stop=k == KD - 1)
                mm.then_inc(prod_ok, 1)
            pe.wait_ge(prod_out, len(UNITS))
            pe.wait_ge(phi_ok, NPHI)
            for j in range(KD):
                c = slice(128 * j, 128 * j + 128)
                if j >= 2:
                    pe.wait_ge(kvb_ok, j - 1)
                for t in range(T):
                    pe.matmul(ps[:, 4 + j % 2, 0:128], K[:, t, c], V[:, t, c], start=t == 0, stop=t == T - 1)
                for t in range(T):
                    mm = pe.matmul(ps[:, 4 + j % 2, 128:256], K[:, t, c], m.ones[0:R, :], start=t == 0, stop=t == T - 1)
                mm.then_inc(kv_ok, 1)
            for u in range(3 * KD):
                j, (c, w), b = u // 3, SPANS[u % 3], 2 * (u % 2)
                pe.wait_ge(kvb_ok, j + 1)
                if u >= 2:
                    pe.wait_ge(yt_ok, u - 1)
                pe.matmul(ps[:, b, 0:w], KVB[:, j, 0, :], QT[:, j, c:c + w], start=True, stop=True)
                pe.matmul(ps[:, b + 1, 0:w], KVB[:, j, 1, :], QT[:, j, c:c + w], start=True, stop=True).then_inc(y_ok, 1)
            pe.wait_ge(yt_ok, 3 * KD)
            for u in range(2 * T):
                s, t = divmod(u, T)
                pe.wait_ge(w_in[s], 16 * 4)
                if u >= 4:
                    pe.wait_ge(o_out, u - 3)
                for k in range(KD):
                    mm = pe.matmul(ps[0:R, 4 + u % 4, 0:384], QT[:, k, R * t:R * t + R], W_SLOT[s][:, k, :],
                                   start=k == 0, stop=k == KD - 1)
                mm.then_inc(o_ok, 1)


def graph_phase(nc, m, io):
    ES = area(m, 125, 2 * QC * CH, QUADS).rearrange("p (a e) -> p a e", a=2)
    EF = area(m, 129, 2 * QC * CH, QUADS).rearrange("p (a e) -> p a e", a=2)
    ET = area(m, 133, 2 * QC * QUADS, CH).rearrange("p (a k q) -> p a k q", a=2, k=QC)
    IOTA = area(m, 136, N // 2, CH).bitcast(U16)
    SRC1 = [area(m, 139 + 2.5 * i, N // 2, CH).bitcast(BF16) for i in range(QC)]
    DST1 = [area(m, 149 + i / 4, 63, CH).bitcast(BF16)[:, 0:R] for i in range(QC)]
    DIAG = area(m, 150, (2 * N - R + 1) // 2, R).bitcast(BF16)
    CT = [area(m, 155 + 5 * i, N, R) for i in range(2)]
    SM = area(m, 165, 128, QUADS)
    BSTART = area(m, 166, T, QUADS)
    QIDX = area(m, 167, 2, QUADS)
    KEYS = area(m, 168, 2 * T, QUADS)
    LOHI = area(m, 169, 2, T)
    BOUNDS = area(m, 170, 2 * T, 1).bitcast(I32)
    C, MT, ps = m.C, m.MT, m.ps

    e_in, graph_const, ef_ok, et_ok, et_out, key_ok = (m.sem(s) for s in ("e_in", "graph_const", "ef_ok", "et_ok", "et_out", "key_ok"))
    keyt_ok, lohi_ok, bound_ok, bounds_ok = (m.sem(s) for s in ("keyt_ok", "lohi_ok", "bound_ok", "bounds_ok"))
    hot_ok, hot_free, ct_ps, ct_ok, mt_ok, c_tr, c_ok = (m.sem(s) for s in ("hot_ok", "hot_free", "ct_ps", "ct_ok", "mt_ok", "c_tr", "c_ok"))
    dve_own = m.sem("dve_own2")
    ROUNDS = [(0, 4), (4, 4), (8, 2)]

    with nc.Block() as block:
        @block.sync
        def _(sp):
            for i, v in enumerate((io.src, io.dst)):
                sp.dma_start(ES[:, i, :].bitcast(I32), v.rearrange("(q e) -> q e", q=QUADS)).then_inc(e_in, 16)

        @block.gpsimd
        def _(pool):
            pool.iota(IOTA, [[1, N]], base=0, channel_multiplier=0).then_inc(graph_const, 1)
            pool.iota(BSTART, [[R, T]], base=0, channel_multiplier=0, allow_small_or_imprecise_dtypes=True).then_inc(graph_const, 1)
            pool.iota(QIDX, [[1, 2]], base=0, channel_multiplier=1, allow_small_or_imprecise_dtypes=True).then_inc(graph_const, 1)
            pool.memset(DIAG, 0.0).then_inc(graph_const, 1)
            pool.wait_ge(graph_const, 4)
            pool.tensor_copy(DIAG[:, N - R:N], m.ident[0:R, 0:R]).then_inc(graph_const, 1)
            for b in range(T):
                pool.wait_ge(ct_ok, 2 * b + 2)
                pool.tensor_scalar(MT[:, b, :], CT[b % 2], 0.0, NEG, ALU.is_equal, ALU.mult).then_inc(mt_ok, 1)

        @block.vector
        def _(dve):
            link = Chain(dve, dve_own)
            dve.wait_ge(e_in, 32)
            link(dve.tensor_copy(EF, ES.bitcast(I32)))
            dve.engine_nop().then_inc(ef_ok, 1)
            lo_d, hi_d, below = SM[:, 0:1], SM[:, 1:2], SM[:, 2:3]
            is_in, tmp = SM[:, 16:26], SM[:, 32:42]
            link(dve.tensor_reduce(lo_d, EF[:, 1, :], AX_X, ALU.min))
            link(dve.tensor_reduce(hi_d, EF[:, 1, :], AX_X, ALU.max))
            link(dve.tensor_scalar(below, lo_d, float(R), None, ALU.subtract))
            dve.wait_ge(graph_const, 5)
            link(dve.tensor_scalar(is_in, BSTART, below, None, ALU.is_gt))
            link(dve.tensor_scalar(tmp, BSTART, hi_d, None, ALU.is_le))
            link(dve.tensor_tensor(is_in, is_in, tmp, ALU.mult))
            link(dve.tensor_scalar(KEYS[:, T:2 * T], is_in, QIDX[:, 1:2], None, ALU.mult))
            link(dve.tensor_scalar(tmp, is_in, QIDX[:, 0:1], float(QUADS), ALU.mult, ALU.add))
            link(dve.tensor_scalar(is_in, is_in, float(QUADS), None, ALU.mult))
            dve.tensor_tensor(KEYS[:, 0:T], tmp, is_in, ALU.subtract).then_inc(key_ok, 1)
            for a in range(2):
                dve.wait_ge(et_ok, a + 1)
                dve.tensor_copy(ET[:, a, :, :], ps[0:CH, a, 0:QC * QUADS].rearrange("p (k q) -> p k q", k=QC)).then_inc(et_out, 1)
            dve.wait_ge(keyt_ok, 1)
            link(dve.tensor_reduce(LOHI[:, 0:1], ps[0:T, 2, 0:QUADS], AX_X, ALU.min))
            link(dve.tensor_reduce(LOHI[:, 1:2], ps[0:T, 2, QUADS:2 * QUADS], AX_X, ALU.max))
            link(dve.tensor_scalar(LOHI[:, 0:1], LOHI[:, 0:1], float(QUADS - 1), None, ALU.min))
            dve.scalar_tensor_tensor(out=LOHI[:, 1:2], in0=LOHI[:, 0:1], scalar=1.0, in1=LOHI[:, 1:2],
                                     op0=ALU.add, op1=ALU.max).then_inc(lohi_ok, 1)
            dve.wait_ge(bound_ok, 1)
            dve.tensor_copy(BOUNDS, ps[0:1, 3, 0:2 * T]).then_inc(bounds_ok, 1)
            dve.wait_ge(bounds_ok, 1)
            dve.wait_ge(et_out, 2)
            chunk = dve.alloc_register("dve_chunk")
            dve.reg_mov(chunk, 0)
            for b in range(T):
                first = dve.value_load(BOUNDS[0:1, b:b + 1], min_val=0, max_val=QUADS - 1)
                end = dve.value_load(BOUNDS[0:1, T + b:T + b + 1], min_val=1, max_val=QUADS)
                with dve.Fori(first, end) as q:
                    for k in range(QC):
                        dve.reg_add(chunk, chunk, 1)
                        dve.wait_ge(hot_free, chunk)
                        dve.tensor_scalar(DST1[k], IOTA[:, R * b:R * b + R], ET[:, 1, k, bass.ds(q, 1)], None, ALU.is_equal)
                        dve.tensor_scalar(SRC1[k], IOTA, ET[:, 0, k, bass.ds(q, 1)], None, ALU.is_equal).then_inc(hot_ok, 1)

        @block.tensor
        def _(pe):
            pe.wait_ge(ef_ok, 1)
            for a in range(2):
                for k in range(QC):
                    tr = pe.transpose(ps[0:CH, a, QUADS * k:QUADS * (k + 1)], EF[:, a, CH * k:CH * (k + 1)],
                                      m.ident[0:QUADS, 0:QUADS])
                tr.then_inc(et_ok, 1)
            pe.wait_ge(key_ok, 1)
            pe.transpose(ps[0:T, 2, 0:QUADS], KEYS[:, 0:T], m.ident[0:QUADS, 0:QUADS])
            pe.transpose(ps[0:T, 2, QUADS:2 * QUADS], KEYS[:, T:2 * T], m.ident[0:QUADS, 0:QUADS]).then_inc(keyt_ok, 1)
            pe.wait_ge(lohi_ok, 1)
            for i in range(2):
                mm = pe.matmul(ps[0:1, 3, T * i:T * (i + 1)], LOHI[:, i:i + 1], m.ident[0:T, 0:T], start=True, stop=True)
            mm.then_inc(bound_ok, 1)
            pe.wait_ge(bounds_ok, 1)
            pe.wait_ge(graph_const, 5)
            pe.wait_ge(et_out, 2)
            pe.nop().then_inc(hot_free, QC)

            def transposes(b):
                for i, (t0, n) in enumerate(ROUNDS):
                    at = 3 * b + i
                    pe.wait_ge(ct_ok, 2 * b + 2)
                    if at >= 2:
                        pe.wait_ge(c_ok, at - 1)
                    for t in range(n):
                        tr = pe.transpose(ps[0:R, 6 + at % 2, R * t:R * t + R], CT[b % 2][:, R * (t0 + t):R * (t0 + t + 1)],
                                          m.ident[0:R, 0:R])
                    tr.then_inc(c_tr, 1)

            chunk = pe.alloc_register("pe_chunk")
            pe.reg_mov(chunk, 0)
            for b in range(T):
                first = pe.value_load(BOUNDS[0:1, b:b + 1], min_val=0, max_val=QUADS - 1)
                end = pe.value_load(BOUNDS[0:1, T + b:T + b + 1], min_val=1, max_val=QUADS)
                banks = [3 * (b % 2) + j for j in range(3)]
                if b >= 2:
                    pe.wait_ge(ct_ok, 2 * (b - 1))
                for j, (c, w) in zip(banks, SPANS):
                    pe.matmul(ps[0:R, j, 0:w], DIAG[:, N - R:N], DIAG[:, 0:w], start=True, stop=False)
                with pe.Fori(first, end) as q:
                    for k in range(QC):
                        pe.reg_add(chunk, chunk, 1)
                        pe.wait_ge(hot_ok, chunk)
                        for j, (c, w) in zip(banks, SPANS):
                            mm = pe.matmul(ps[0:R, j, 0:w], DST1[k], SRC1[k][:, c:c + w], start=False, stop=False)
                        mm.then_inc(hot_free, 1)
                for j, (c, w) in zip(banks, SPANS):
                    at = N - R - R * b + c
                    mm = pe.matmul(ps[0:R, j, 0:w], DIAG[:, N - R:N], DIAG[:, at:at + w], start=False, stop=True)
                mm.then_inc(ct_ps, 1)
                if b >= 1:
                    transposes(b - 1)
            transposes(T - 1)

        @block.scalar
        def _(act):
            def copy_c(b):
                for i, (t0, n) in enumerate(ROUNDS):
                    at = 3 * b + i
                    act.wait_ge(c_tr, at + 1)
                    act.copy(C[:, t0:t0 + n, R * b:R * b + R],
                             ps[0:R, 6 + at % 2, 0:R * n].rearrange("p (t n) -> p t n", t=n)).then_inc(c_ok, 1)

            for b in range(T):
                j = 3 * (b % 2)
                act.wait_ge(ct_ps, b + 1)
                if b >= 2:
                    act.wait_ge(mt_ok, b - 1)
                    act.wait_ge(c_tr, 3 * (b - 1))
                act.copy(CT[b % 2][:, 0:1000].rearrange("p (j n) -> p j n", j=2), ps[0:R, j:j + 2, 0:500]).then_inc(ct_ok, 1)
                act.copy(CT[b % 2][:, 1000:N], ps[0:R, j + 2, 0:250]).then_inc(ct_ok, 1)
                if b >= 1:
                    copy_c(b - 1)
            copy_c(T - 1)


class Attention:

    def __init__(self, m, name, heads, width, XL):
        self.m, self.heads, self.width, self.XL = m, heads, width, XL
        self.ngroups = heads * len(GROUPS)
        self.P = [area(m, 50 + 20 * i, T * 500, R).rearrange("p (t n) -> p t n", t=T) for i in range(2)]
        self.WK = [area(m, 171 + 2 * i, 500, R) for i in range(4)]
        self.DG = [area(m, 179 + 2 * i, 500, R) for i in range(2)]
        self.ASB = area(m, 183, N, R)
        self.JUNK = area(m, 188, N // 2, R).bitcast(BF16)
        self.MB = [area(m, 191 + 2 * i, 500, R) for i in range(2)]
        sm = area(m, 190.5, 128, R)
        self.MX, self.Z = sm[:, 0:T], sm[:, T:2 * T]
        self.M = sm[:, 42:52]
        self.ADM = [sm[:, 20:30], sm[:, 30:40]]
        self.DEN = sm[:, 40:42]
        sem = {s: m.sem(f"{name}_{s}") for s in ("score_ok", "dg_ok", "spread_ok", "asb_ok", "max_ok", "lre_ok",
                                                 "mb_ok", "sub_ok", "e_ok", "p_ok", "agg_ok", "agg_out")}
        self.score_ok, self.dg_ok, self.spread_ok = sem["score_ok"], sem["dg_ok"], sem["spread_ok"]
        self.asb_ok, self.max_ok, self.mb_ok = sem["asb_ok"], sem["max_ok"], sem["mb_ok"]
        self.lre_ok, self.sub_ok, self.e_ok, self.p_ok = sem["lre_ok"], sem["sub_ok"], sem["e_ok"], sem["p_ok"]
        self.agg_ok, self.agg_out = sem["agg_ok"], sem["agg_out"]
        self.nb = 1 if width + 1 <= 512 else 2
        self.spreads = [("as", 0, j) for j in range(3)] + [("ad", 0), ("m", 0)]
        for g in range(self.ngroups):
            if g + 1 < self.ngroups:
                self.spreads += [("ad", g + 1), ("m", g + 1)]
            if g % 3 == 0 and g // 3 + 1 < heads:
                self.spreads += [("as", g // 3 + 1, j) for j in range(3)]
        self.order = {s: i for i, s in enumerate(self.spreads)}

    def columns(self, g):
        t0, n = GROUPS[g % 3]
        return g // 3, t0, n

    def tiles_to(self, g):
        return T * (g // 3) + GROUPS[g % 3][0]

    def pool_diagonal(self, pool, s):
        m, i = self.m, self.order[s]
        if s[0] == "as":
            c, w = SPANS[s[2]]
            n, v = w // R, m.AS[:, s[1], c // R:(c + w) // R]
            pool.wait_ge(self.score_ok, s[1] + 1)
        else:
            h, t0, n = self.columns(s[1])
            if s[0] == "ad":
                v = m.AD[:, h, t0:t0 + n]
            else:
                v = self.ADM[h % 2][:, t0:t0 + n]
                pool.wait_ge(self.max_ok, h + 1)
        if i >= 2:
            pool.wait_ge(self.spread_ok, i - 1)
        pool.tensor_tensor(self.DG[i % 2][:, 0:R * n].rearrange("p (t n) -> p t n", t=n),
                           m.ident[0:R, 0:R].unsqueeze(1).broadcast_to([R, n, R]),
                           v.unsqueeze(2).broadcast_to([R, n, R]), ALU.mult).then_inc(self.dg_ok, 1)

    def pool(self, pool):
        for s in self.spreads[0:5]:
            self.pool_diagonal(pool, s)
        for g in range(self.ngroups):
            h, t0, n = self.columns(g)
            pool.wait_ge(self.mb_ok, g + 1)
            for t in range(T):
                at = T * g + t
                wk = self.WK[at % 4][:, 0:R * n]
                pool.wait_ge(self.lre_ok, at + 1)
                pool.tensor_tensor(wk, wk, self.MB[g % 2][:, 0:R * n], ALU.add).then_inc(self.sub_ok, 1)
                if g % 3 == 1 and h + 1 < self.heads and t in (2, 4, 6):
                    self.pool_diagonal(pool, ("as", h + 1, t // 2 - 1))
            if g + 1 < self.ngroups:
                self.pool_diagonal(pool, ("ad", g + 1))
                self.pool_diagonal(pool, ("m", g + 1))

    def act_scores(self, act, h, j):
        c, w = SPANS[j]
        act.wait_ge(self.spread_ok, self.order[("as", h, j)] + 1)
        if h >= 1:
            act.wait_ge(self.max_ok, h)
        act.copy(self.ASB[:, c:c + w], self.m.ps[0:R, 2 + j % 2, 0:w]).then_inc(self.asb_ok, 1)

    def act(self, act):
        m = self.m

        def lrelu(g, t):
            h, t0, n = self.columns(g)
            at = T * g + t
            if at >= 4:
                act.wait_ge(self.p_ok, at - 3)
            act.activation(self.WK[at % 4][:, 0:R * n], m.ps[0:R, 4 + 2 * (g % 2), 0:R * n], ACT.Relu,
                           bias=m.AS8[:, h, t:t + 1], scale=0.8).then_inc(self.lre_ok, 1)

        for g in range(self.ngroups):
            h, t0, n = self.columns(g)
            act.wait_ge(self.spread_ok, self.order[("m", g)] + 1)
            act.copy(self.MB[g % 2][:, 0:R * n], m.ps[0:R, 5 + 2 * (g % 2), 0:R * n]).then_inc(self.mb_ok, 1)
            lrelu(g, 0)
            lrelu(g, 1)
            for t in range(T):
                at = T * g + t
                if t + 2 < T:
                    lrelu(g, t + 2)
                wk = self.WK[at % 4][:, 0:R * n]
                act.wait_ge(self.sub_ok, at + 1)
                act.activation(wk, wk, ACT.Exp, bias=m.AS2[:, h, t:t + 1]).then_inc(self.e_ok, 1)
                if g % 3 == 1 and h + 1 < self.heads and t in (3, 5, 7):
                    self.act_scores(act, h + 1, (t - 3) // 2)

    def dve_max_step(self, dve, link, h, t):
        if t == 0:
            dve.wait_ge(self.asb_ok, 3 * (h + 1))
        link(dve.tensor_tensor_reduce(out=self.JUNK, in0=self.m.MT[:, t, :], in1=self.ASB, scale=1.0, scalar=2 * NEG,
                                      op0=ALU.add, op1=ALU.max, accum_out=self.MX[:, t:t + 1]))

    def dve_maxima(self, dve, link, h):
        link(dve.tensor_tensor(self.Z, self.MX, self.m.AD[:, h, :], ALU.add))
        link(dve.scalar_tensor_tensor(out=self.M, in0=self.Z, scalar=0.2, in1=self.Z, op0=ALU.mult, op1=ALU.max))
        dve.scalar_tensor_tensor(out=self.ADM[h % 2], in0=self.m.AD[:, h, :], scalar=0.2, in1=self.M, op0=ALU.mult,
                                 op1=ALU.subtract).then_inc(self.max_ok, 1)

    def dve(self, dve, link, finish):
        for t in range(T):
            self.dve_max_step(dve, link, 0, t)
        self.dve_maxima(dve, link, 0)
        for g in range(self.ngroups + 1):
            behind = self.columns(g - 1)[2] if g else 0
            out = 0
            makes = g < self.ngroups
            next_head = makes and g % 3 == 2 and g + 1 < self.ngroups
            if makes:
                h, t0, n = self.columns(g)
                if g >= 2:
                    dve.wait_ge(self.agg_ok, self.tiles_to(g - 1))
            for t in range(T):
                if makes:
                    at = T * g + t
                    dve.wait_ge(self.e_ok, at + 1)
                    dve.tensor_tensor(self.P[g % 2][:, t, 0:R * n], self.WK[at % 4][:, 0:R * n],
                                      self.m.C[:, t, R * t0:R * (t0 + n)], ALU.mult).then_inc(self.p_ok, 1)
                if next_head:
                    self.dve_max_step(dve, link, h + 1, t)
                while out < behind and (out + 1) * T <= (t + 1) * behind:
                    finish(self.tiles_to(g - 1) + out)
                    out += 1
            if next_head:
                self.dve_maxima(dve, link, h + 1)

    def pe_spread(self, pe, s):
        m, i = self.m, self.order[s]
        pe.wait_ge(self.dg_ok, i + 1)
        if s[0] == "as":
            w, bank = SPANS[s[2]][1], 2 + s[2] % 2
            copied = 3 * s[1] + (1 if s[2] == 2 else 0)
            if copied:
                pe.wait_ge(self.asb_ok, copied)
        else:
            g = s[1]
            w, bank = R * self.columns(g)[2], 4 + 2 * (g % 2) + (s[0] == "m")
            if g >= 2:
                pe.wait_ge(*((self.mb_ok, g - 1) if s[0] == "m" else (self.lre_ok, T * (g - 1))))
        pe.matmul(m.ps[0:R, bank, 0:w], m.ones[0:R, 0:R], self.DG[i % 2][:, 0:w], start=True, stop=True)\
          .then_inc(self.spread_ok, 1)

    def pe(self, pe):
        m = self.m
        self.pe_spread(pe, ("ad", 0))
        self.pe_spread(pe, ("m", 0))
        for g in range(self.ngroups):
            h, t0, n = self.columns(g)
            if g + 1 < self.ngroups:
                self.pe_spread(pe, ("ad", g + 1))
                self.pe_spread(pe, ("m", g + 1))
            for i in range(n):
                tile = self.tiles_to(g) + i
                if tile >= 2:
                    pe.wait_ge(self.agg_out, tile - 1)
                for b in range(self.nb):
                    c, w = (0, self.width + 1) if self.nb == 1 else ((0, 384), (384, 385))[b]
                    bank = (tile % 2) * self.nb + b
                    for t in range(T):
                        if i == 0 and b == 0:
                            pe.wait_ge(self.p_ok, T * g + t + 1)
                        mm = pe.matmul(m.ps[0:R, bank, 0:w], self.P[g % 2][:, t, R * i:R * i + R],
                                       self.XL(h, t)[:, c:c + w], start=t == 0, stop=t == T - 1)
                mm.then_inc(self.agg_ok, 1)
                if g % 3 == 0 and h + 1 < self.heads and i < 3:
                    self.pe_spread(pe, ("as", h + 1, i))


def gat1_phase(nc, m, io):
    XL = area(m, 130, HEADS * T * (HID + 1), R).rearrange("p (h t c) -> p h t c", h=HEADS, t=T)
    H = area(m, 90, T * HC, R).rearrange("p (t c) -> p t c", t=T)
    W_SLOT = [area(m, 60 + 6 * i, KD * HID).rearrange("p (k c) -> p k c", k=KD) for i in range(2)]
    A_ROWS = area(m, 50, 2 * HC, R)
    TJ = area(m, 58, HID, R)
    ST = [area(m, 195 + i, HID, R) for i in range(2)]
    XNT, ps = m.XNT, m.ps
    att = Attention(m, "gat1", HEADS, HID, lambda h, t: XL[:, h, t, :])
    a_in, ones_ok, w_in = m.sem("a1_in"), m.sem("xl1_ones"), m.sems("w1_in", 2)
    prod_ok, prod_out, r1_out, own = m.sem("prod1_ok"), m.sem("prod1_out"), m.sems("r1_out", 2), m.sem("dve_own3")
    UNITS = [(s, t) for s in range(2 * HEADS) for t in range(T)]

    with nc.Block() as block:
        @block.sync
        def _(sp):
            def store_r1(i):
                for u in range(T * i, T * (i + 1)):
                    sp.wait_ge(prod_out, T * HEADS + u + 1)
                    sp.dma_start(m.r1_d[u % T * R:(u % T + 1) * R, HID * i:HID * (i + 1)], ST[u % 2]).then_inc(r1_out[u % 2], 16)

            for i in range(2 * HEADS):
                if i - 2 >= HEADS:
                    store_r1(i - 2 - HEADS)
                if i >= 2:
                    sp.wait_ge(prod_ok, T * (i - 1))
                w = io.W1 if i < HEADS else io.Wr1
                sp.dma_start(W_SLOT[i % 2], slab_of(w, HID * (i % HEADS), HID)).then_inc(w_in[i % 2], 16)
                if i == 0:
                    sp.dma_start(A_ROWS[:, 0:HC], rows_of(io.a_src1.rearrange("h c -> (h c)"))).then_inc(a_in, 16)
                    sp.dma_start(A_ROWS[:, HC:2 * HC], rows_of(io.a_dst1.rearrange("h c -> (h c)"))).then_inc(a_in, 16)
            for i in range(HEADS - 2, HEADS):
                store_r1(i)
            for i in range(2):
                sp.wait_ge(r1_out[i], 16 * T * HEADS // 2)

        @block.gpsimd
        def _(pool):
            pool.memset(XL[:, :, :, HID:HID + 1], 1.0).then_inc(ones_ok, 1)
            att.pool(pool)

        @block.scalar
        def _(act):
            def projections():
                for u, (s, t) in enumerate(UNITS):
                    if u == T * HEADS:
                        for j in range(3):
                            att.act_scores(act, 0, j)
                    act.wait_ge(prod_ok, u + 1)
                    if s < HEADS:
                        act.copy(XL[:, s, t, 0:HID], ps[0:R, u % 2, 0:HID]).then_inc(prod_out, 1)
                    else:
                        if u >= T * HEADS + 2:
                            act.wait_ge(r1_out[u % 2], 16 * ((u - T * HEADS) // 2))
                        act.copy(ST[u % 2], ps[0:R, u % 2, 0:HID]).then_inc(prod_out, 1)

            projections()
            att.act(act)

        @block.vector
        def _(dve):
            link = Chain(dve, own)
            dve.wait_ge(a_in, 32)
            for h in range(HEADS):
                for t in range(T):
                    dve.wait_ge(prod_out, T * h + t + 1)
                    for i, col in ((0, m.AS), (1, m.AD)):
                        c = HC * i + HID * h
                        link(dve.tensor_tensor_reduce(out=TJ, in0=XL[:, h, t, 0:HID], in1=A_ROWS[:, c:c + HID], scale=1.0,
                                                      scalar=0.0, op0=ALU.mult, op1=ALU.add, accum_out=col[:, h, t:t + 1]))
                dve.tensor_scalar(m.AS8[:, h, :], m.AS[:, h, :], 0.8, None, ALU.mult)
                dve.tensor_scalar(m.AS2[:, h, :], m.AS[:, h, :], 0.2, None, ALU.mult).then_inc(att.score_ok, 1)

            def finish(tile):
                h, t = divmod(tile, T)
                dve.wait_ge(att.agg_ok, tile + 1)
                link(dve.tensor_scalar(att.DEN[:, 0:1], ps[0:R, tile % 2, HID:HID + 1], 1e-16, None, ALU.add))
                link(dve.reciprocal(att.DEN[:, 1:2], att.DEN[:, 0:1]))
                dve.tensor_scalar(H[:, t, HID * h:HID * (h + 1)], ps[0:R, tile % 2, 0:HID], att.DEN[:, 1:2], None,
                                  ALU.mult).then_inc(att.agg_out, 1)

            att.dve(dve, link, finish)

        @block.tensor
        def _(pe):
            for u, (s, t) in enumerate(UNITS):
                if u == T * HEADS:
                    for j in range(3):
                        att.pe_spread(pe, ("as", 0, j))
                pe.wait_ge(w_in[s % 2], 16 * (s // 2 + 1))
                if u >= 2:
                    pe.wait_ge(prod_out, u - 1)
                for k in range(KD):
                    mm = pe.matmul(ps[0:R, u % 2, 0:HID], XNT[:, k, R * t:R * t + R], W_SLOT[s % 2][:, k, :],
                                   start=k == 0, stop=k == KD - 1)
                mm.then_inc(prod_ok, 1)
            pe.wait_ge(prod_out, len(UNITS))
            pe.wait_ge(ones_ok, 1)
            att.pe(pe)


def gat2_phase(nc, m, io):
    H = area(m, 90, T * HC, R).rearrange("p (t c) -> p t c", t=T)
    H1T = area(m, 130, KH * N).rearrange("p (k n) -> p k n", k=KH)
    ROWS = area(m, 50, 4 * HC, R)
    R1 = [area(m, 66 + 4 * i, HC, R) for i in range(2)]
    WC = 256
    NS = D // WC
    W_SLOT = [area(m, 74 + 8 * i, KH * WC).rearrange("p (k c) -> p k c", k=KH) for i in range(2)]
    ST = [area(m, 195 + i, WC, R) for i in range(2)]
    XL = area(m, 90, T * (D + 1), R).rearrange("p (t c) -> p t c", t=T)
    A_ROWS = area(m, 120.25, 2 * D, R)
    TJ = area(m, 126.5, D, R)
    H2 = area(m, 127, T * D, R).rearrange("p (t c) -> p t c", t=T)
    ps = m.ps
    att = Attention(m, "gat2", 1, D, lambda h, t: XL[:, t, :])
    row_in, r1_in, w_in, a_in, ones_ok = m.sem("row1_in"), m.sems("r1_in", 2), m.sems("w2_in", 2), m.sem("a2_in"), m.sem("xl2_ones")
    hb_ok, rb_ok, mv_ok, sd_ok, h1_ok, ht_ok, h1t_ok = (
        m.sem(s) for s in ("hb_ok", "rb_ok", "mv1_ok", "sd1_ok", "h1_ok", "ht_ok", "h1t_ok"))
    prod_ok, prod_out, r2_out, own = m.sem("prod2_ok"), m.sem("prod2_out"), m.sems("r2_out", 2), m.sem("dve_own4")
    UNITS = [(s, t) for s in range(2 * NS) for t in range(T)]

    def row(i):
        return ROWS[:, HC * i:HC * (i + 1)]

    with nc.Block() as block:
        @block.sync
        def _(sp):
            for i, v in enumerate((io.b1, io.g1, io.be1, io.br1)):
                sp.dma_start(row(i), rows_of(v)).then_inc(row_in, 16)
            for i in range(2):
                sp.dma_start(W_SLOT[i], slab_of(io.W2, WC * i, WC)).then_inc(w_in[i], 16)
            for t in range(T):
                if t >= 2:
                    sp.wait_ge(h1_ok, t - 1)
                sp.dma_start(R1[t % 2], tile_rows(m.r1_d, t)).then_inc(r1_in[t % 2], 16)
            sp.wait_ge(ht_ok, 2 * T)
            for i, v in enumerate((io.a_src2, io.a_dst2)):
                sp.dma_start(A_ROWS[:, D * i:D * (i + 1)], rows_of(v.rearrange("h c -> (h c)"))).then_inc(a_in, 16)
            def store_r2(i):
                for u in range(T * i, T * (i + 1)):
                    sp.wait_ge(prod_out, T * NS + u + 1)
                    sp.dma_start(m.r2_d[u % T * R:(u % T + 1) * R, WC * i:WC * (i + 1)], ST[u % 2]).then_inc(r2_out[u % 2], 16)

            for i in range(2, 2 * NS):
                if i - 2 >= NS:
                    store_r2(i - 2 - NS)
                sp.wait_ge(prod_ok, T * (i - 1))
                w = io.W2 if i < NS else io.Wr2
                sp.dma_start(W_SLOT[i % 2], slab_of(w, WC * (i % NS), WC)).then_inc(w_in[i % 2], 16)
            for i in range(NS - 2, NS):
                store_r2(i)
            for i in range(2):
                sp.wait_ge(r2_out[i], 16 * T * NS // 2)

        @block.gpsimd
        def _(pool):
            pool.wait_ge(row_in, 64)
            for t in range(T):
                pool.tensor_tensor(H[:, t, :], H[:, t, :], row(0), ALU.add).then_inc(hb_ok, 1)
                pool.wait_ge(r1_in[t % 2], 16 * (t // 2 + 1))
                pool.tensor_tensor(R1[t % 2], R1[t % 2], row(3), ALU.add).then_inc(rb_ok, 1)
            pool.wait_ge(ht_ok, 2 * T)
            pool.memset(XL[:, :, D:D + 1], 1.0).then_inc(ones_ok, 1)
            att.pool(pool)

        @block.scalar
        def _(act):
            def copy_h1(t):
                for j in range(2):
                    act.wait_ge(ht_ok, 2 * t + j + 1)
                    act.copy(H1T[:, 4 * j:4 * j + 4, R * t:R * t + R],
                             ps[:, 2 + 2 * (t % 2) + j, 0:4 * R].rearrange("p (k n) -> p k n", k=4)).then_inc(h1t_ok, 1)

            def projections():
                for t in range(T):
                    act.wait_ge(mv_ok, t + 1)
                    act.activation(m.sd[0:R, t:t + 1], m.mv[0:R, t, 1:2], ACT.Sqrt, bias=m.eps[0:R, :]).then_inc(sd_ok, 1)
                    if t >= 1:
                        copy_h1(t - 1)
                copy_h1(T - 1)
                for u, (s, t) in enumerate(UNITS):
                    if u == T * NS:
                        for j in range(3):
                            att.act_scores(act, 0, j)
                    act.wait_ge(prod_ok, u + 1)
                    if s < NS:
                        act.copy(XL[:, t, WC * s:WC * (s + 1)], ps[0:R, u % 2, 0:WC]).then_inc(prod_out, 1)
                    else:
                        if u >= T * NS + 2:
                            act.wait_ge(r2_out[u % 2], 16 * ((u - T * NS) // 2))
                        act.copy(ST[u % 2], ps[0:R, u % 2, 0:WC]).then_inc(prod_out, 1)

            projections()
            att.act(act)

        @block.vector
        def _(dve):
            link = Chain(dve, own)
            dve.wait_ge(row_in, 64)

            def rest(t):
                h = H[:, t, :]
                dve.wait_ge(sd_ok, t + 1)
                link(dve.reciprocal(m.rstd[0:R, t:t + 1], m.sd[0:R, t:t + 1]))
                link(dve.tensor_scalar(h, h, m.mv[0:R, t, 0:1], m.rstd[0:R, t:t + 1], ALU.subtract, ALU.mult))
                link(dve.tensor_tensor(h, h, row(1), ALU.mult))
                link(dve.tensor_tensor(h, h, row(2), ALU.add))
                dve.wait_ge(rb_ok, t + 1)
                dve.scalar_tensor_tensor(out=h, in0=h, scalar=0.0, in1=R1[t % 2], op0=ALU.max, op1=ALU.add).then_inc(h1_ok, 1)

            for t in range(T):
                dve.wait_ge(hb_ok, t + 1)
                moments(dve, link, m.stats, t, H[:, t, :], m.mv, mv_ok)
                if t >= 1:
                    rest(t - 1)
            rest(T - 1)
            dve.wait_ge(a_in, 32)
            for t in range(T):
                dve.wait_ge(prod_out, T * (NS - 1) + t + 1)
                for i, col in ((0, m.AS), (1, m.AD)):
                    link(dve.tensor_tensor_reduce(out=TJ, in0=XL[:, t, 0:D], in1=A_ROWS[:, D * i:D * (i + 1)], scale=1.0,
                                                  scalar=0.0, op0=ALU.mult, op1=ALU.add, accum_out=col[:, 0, t:t + 1]))
            dve.tensor_scalar(m.AS8[:, 0, :], m.AS[:, 0, :], 0.8, None, ALU.mult)
            dve.tensor_scalar(m.AS2[:, 0, :], m.AS[:, 0, :], 0.2, None, ALU.mult).then_inc(att.score_ok, 1)

            def finish(t):
                b = 2 * (t % 2)
                dve.wait_ge(att.agg_ok, t + 1)
                link(dve.tensor_scalar(att.DEN[:, 0:1], ps[0:R, b + 1, 384:385], 1e-16, None, ALU.add))
                link(dve.reciprocal(att.DEN[:, 1:2], att.DEN[:, 0:1]))
                dve.tensor_scalar(H2[:, t, :].rearrange("p (j c) -> p j c", j=2), ps[0:R, b:b + 2, 0:384], att.DEN[:, 1:2],
                                  None, ALU.mult).then_inc(att.agg_out, 1)

            att.dve(dve, link, finish)

        @block.tensor
        def _(pe):
            for t in range(T):
                pe.wait_ge(h1_ok, t + 1)
                for j in range(2):
                    if t >= 2:
                        pe.wait_ge(h1t_ok, 2 * (t - 2) + j + 1)
                    for k in range(4):
                        tr = pe.transpose(ps[:, 2 + 2 * (t % 2) + j, R * k:R * k + R],
                                          H[:, t, (4 * j + k) * 128:(4 * j + k + 1) * 128], m.ident[0:R, 0:R])
                    tr.then_inc(ht_ok, 1)
            for u, (s, t) in enumerate(UNITS):
                if u == T * NS:
                    for j in range(3):
                        att.pe_spread(pe, ("as", 0, j))
                pe.wait_ge(w_in[s % 2], 16 * (s // 2 + 1))
                if u >= 2:
                    pe.wait_ge(prod_out, u - 1)
                pe.wait_ge(h1t_ok, 2 * min(t + 1, T))
                for k in range(KH):
                    mm = pe.matmul(ps[0:R, u % 2, 0:WC], H1T[:, k, R * t:R * t + R], W_SLOT[s % 2][:, k, :],
                                   start=k == 0, stop=k == KH - 1)
                mm.then_inc(prod_ok, 1)
            pe.wait_ge(prod_out, len(UNITS))
            pe.wait_ge(ones_ok, 1)
            att.pe(pe)


def ffn_phase(nc, m, io):
    X1 = area(m, 0, T * D, R).rearrange("p (t c) -> p t c", t=T)
    X2T = area(m, 30, KD * N).rearrange("p (k n) -> p k n", k=KD)
    W1S = [area(m, 60 + 9 * i, KD * H_FFN).rearrange("p (k c) -> p k c", k=KD) for i in range(2)]
    XN = [area(m, 78 + 3 * i, D, R) for i in range(2)]
    MASK = area(m, 78, E_FFN * N).rearrange("p (e n) -> p e n", e=E_FFN)
    ROWS = area(m, 98, 4 * D, R)
    R2 = [area(m, 110 + 3 * i, D, R) for i in range(2)]
    RES = [area(m, 116 + 3 * i, D, R) for i in range(2)]
    H2 = area(m, 127, T * D, R).rearrange("p (t c) -> p t c", t=T)
    HT = area(m, 98, E_FFN * KF * N).rearrange("p (g n) -> p g n", g=E_FFN * KF)
    W2F = area(m, 157, E_FFN * KF * D).rearrange("p (g c) -> p g c", g=E_FFN * KF)
    B1C = area(m, 193, E_FFN * KF)
    GW = area(m, 193.25, KD * E_FFN).rearrange("p (k e) -> p k e", k=KD)
    GB = area(m, 193.5, 2 * E_FFN, R)
    SC = area(m, 193.75, T * E_FFN, R).rearrange("p (t e) -> p t e", t=T)
    OH = area(m, 194, T * E_FFN, R).rearrange("p (t e) -> p t e", t=T)
    MXS = area(m, 194.25, 2 * T, R)
    SEL = area(m, 194.5, E_FFN * 128, E_FFN).rearrange("p (e c) -> p e c", e=E_FFN)
    B2F = area(m, 196.5, D, E_FFN)
    OHT = area(m, 199.5, N, E_FFN)
    ps = m.ps

    row_in, p_in, w1_in, w2_in, out_d = m.sem("row2_in"), m.sems("part_in", 2), m.sems("wf1_in", 2), m.sem("wf2_in"), m.sem("out_stored")
    rr_ok, hb_ok, mv_ok, sd_ok, x1_ok, mw_ok, sw_ok, xn_ok, xt_ok, x2_ok = (
        m.sem(s) for s in ("rr_ok", "hb2_ok", "mv2_ok", "sd2_ok", "x1_ok", "mw_ok", "sw_ok", "xn2_ok", "xt2_ok", "x2_ok"))
    gate_ok, oh_ok, oht_ps, oht_ok, sel_ok, mask_ps, mask_ok = (
        m.sem(s) for s in ("gate_ok", "oh_ok", "oht_ps", "oht_ok", "sel_ok", "mask_ps", "mask_ok"))
    up_ok, gelu_ok, ht_ok, down_ok, out_ok, own = (m.sem(s) for s in ("up_ok", "gelu_ok", "hm_ok", "down_ok", "out_ok", "dve_own5"))
    G = E_FFN * KF
    UP = [(g, j) for g in range(G) for j in range(3)]

    def row(i):
        return ROWS[:, D * i:D * (i + 1)]

    with nc.Block() as block:
        @block.sync
        def _(sp):
            for i, v in enumerate((io.b2, io.g2, io.be2, io.br2)):
                sp.dma_start(row(i), rows_of(v)).then_inc(row_in, 16)
            sp.dma_start(GW, io.gate_w.rearrange("(k p) e -> p k e", p=128)).then_inc(row_in, 16)
            sp.dma_start(GB[:, 0:E_FFN], rows_of(io.gate_b)).then_inc(row_in, 16)
            sp.dma_start(GB[:, E_FFN:2 * E_FFN], rows_of(io.gate_center)).then_inc(row_in, 16)
            sp.dma_start(B2F, io.fb2).then_inc(row_in, 16)
            with nc.allow_non_contiguous_dma(reason="1536 words, once"):
                sp.dma_start(B1C, io.fb1.rearrange("e (k p) -> p (e k)", p=128)).then_inc(row_in, 16)
            for e in range(2):
                sp.dma_start(W1S[e], io.w1[e].rearrange("(k p) c -> p k c", p=128)).then_inc(w1_in[e], 16)
            for t in range(T):
                if t >= 2:
                    sp.wait_ge(x1_ok, t - 1)
                sp.dma_start(R2[t % 2], tile_rows(m.r2_d, t)).then_inc(p_in[t % 2], 16)
                sp.dma_start(RES[t % 2], tile_rows(m.res_d, t)).then_inc(p_in[t % 2], 16)
            for e in range(E_FFN):
                sp.dma_start(W2F[:, KF * e:KF * (e + 1), :], io.w2[e].rearrange("(k p) c -> p k c", p=128)).then_inc(w2_in, 16)
            for e in range(2, E_FFN):
                sp.wait_ge(up_ok, 3 * KF * (e - 1))
                sp.dma_start(W1S[e % 2], io.w1[e].rearrange("(k p) c -> p k c", p=128)).then_inc(w1_in[e % 2], 16)
            for t in range(T):
                sp.wait_ge(out_ok, T + t + 1)
                sp.dma_start(tile_rows(io.out, t), X1[:, t, :]).then_inc(out_d, 16)
            sp.wait_ge(out_d, 16 * T)

        @block.gpsimd
        def _(pool):
            pool.wait_ge(row_in, 16 * 9)
            pool.tensor_tensor(row(3), row(3), row(2), ALU.add).then_inc(rr_ok, 1)
            pool.wait_ge(rr_ok, 1)
            for t in range(T):
                pool.tensor_tensor(H2[:, t, :], H2[:, t, :], row(0), ALU.add).then_inc(hb_ok, 1)
                pool.wait_ge(p_in[t % 2], 32 * (t // 2 + 1))
                pool.tensor_tensor(R2[t % 2], R2[t % 2], RES[t % 2], ALU.add).then_inc(rr_ok, 1)
                pool.wait_ge(rr_ok, 2 * t + 2)
                pool.tensor_tensor(R2[t % 2], R2[t % 2], row(3), ALU.add).then_inc(rr_ok, 1)

        @block.scalar
        def _(act):
            def copy_x2(t):
                for j in range(2):
                    act.wait_ge(xt_ok, 2 * t + j + 1)
                    act.copy(X2T[:, 3 * j:3 * j + 3, R * t:R * t + R],
                             ps[:, 2 * (t % 2) + j, 0:3 * R].rearrange("p (k n) -> p k n", k=3)).then_inc(x2_ok, 1)

            for t in range(T + 1):
                if t < T:
                    act.wait_ge(mv_ok, t + 1)
                    act.activation(m.sd[0:R, t:t + 1], m.mv[0:R, t, 1:2], ACT.Sqrt, bias=m.eps[0:R, :]).then_inc(sd_ok, 1)
                if t >= 1:
                    act.wait_ge(mw_ok, t)
                    act.activation(m.sw[0:R, t - 1:t], m.mw[0:R, t - 1, 1:2], ACT.Sqrt, bias=m.eps[0:R, :]).then_inc(sw_ok, 1)
                if t >= 2:
                    copy_x2(t - 2)
            copy_x2(T - 1)
            for i in range(3 * E_FFN):
                e, (c, w) = i // 3, SPANS[i % 3]
                act.wait_ge(mask_ps, i + 1)
                act.copy(MASK[:, e, c:c + w], ps[:, i % 2, 0:w]).then_inc(mask_ok, 1)
            for u, (g, j) in enumerate(UP):
                c, w = SPANS[j]
                act.wait_ge(up_ok, u + 1)
                act.activation(HT[:, g, c:c + w], ps[:, 2 + u % 2, 0:w], ACT.Gelu, bias=B1C[:, g:g + 1]).then_inc(gelu_ok, 1)

        @block.vector
        def _(dve):
            link = Chain(dve, own)
            dve.wait_ge(row_in, 16 * 9)
            for e in range(E_FFN):
                dve.tensor_scalar(SEL[:, e, :], m.ones[0:E_FFN, :], m.ident[0:E_FFN, e:e + 1], None, ALU.mult).then_inc(sel_ok, 1)

            def x1_tile(t):
                h = H2[:, t, :]
                dve.wait_ge(sd_ok, t + 1)
                link(dve.reciprocal(m.rstd[0:R, t:t + 1], m.sd[0:R, t:t + 1]))
                link(dve.tensor_scalar(h, h, m.mv[0:R, t, 0:1], m.rstd[0:R, t:t + 1], ALU.subtract, ALU.mult))
                link(dve.tensor_tensor(h, h, row(1), ALU.mult))
                dve.wait_ge(rr_ok, 2 * t + 3)
                dve.tensor_tensor(X1[:, t, :], h, R2[t % 2], ALU.add).then_inc(x1_ok, 1)
                dve.wait_ge(x1_ok, t + 1)
                moments(dve, link, m.wstats, t, X1[:, t, :], m.mw, mw_ok)

            def xn_tile(t):
                dve.wait_ge(sw_ok, t + 1)
                link(dve.reciprocal(m.rw[0:R, t:t + 1], m.sw[0:R, t:t + 1]))
                if t >= 2:
                    dve.wait_ge(xt_ok, 2 * (t - 1))
                dve.tensor_scalar(XN[t % 2], X1[:, t, :], m.mw[0:R, t, 0:1], m.rw[0:R, t:t + 1], ALU.subtract,
                                  ALU.mult).then_inc(xn_ok, 1)

            for t in range(T + 2):
                if t < T:
                    dve.wait_ge(hb_ok, t + 1)
                    moments(dve, link, m.stats, t, H2[:, t, :], m.mv, mv_ok)
                if 1 <= t <= T:
                    x1_tile(t - 1)
                if t >= 2:
                    xn_tile(t - 2)
            link(dve.tensor_tensor(GB[:, 0:E_FFN], GB[:, 0:E_FFN], GB[:, E_FFN:2 * E_FFN], ALU.subtract))
            dve.wait_ge(gate_ok, 1)
            link(dve.tensor_tensor(SC, ps[0:R, 4, 0:T * E_FFN].rearrange("p (t e) -> p t e", t=T),
                                   GB[:, 0:E_FFN].unsqueeze(1).broadcast_to([R, T, E_FFN]), ALU.add))
            best, taken = MXS[:, 0:T], MXS[:, T:2 * T]
            link(dve.tensor_reduce(best, SC, AX_X, ALU.max))
            link(dve.tensor_tensor(SC, SC, best.unsqueeze(2).broadcast_to([R, T, E_FFN]), ALU.is_equal))
            link(dve.tensor_copy(taken, SC[:, :, 0]))
            link(dve.tensor_copy(OH[:, :, 0], SC[:, :, 0]))
            for e in range(1, E_FFN):
                link(dve.tensor_tensor(OH[:, :, e], taken, SC[:, :, e], ALU.is_lt))
                link(dve.tensor_tensor(taken, taken, SC[:, :, e], ALU.max))
            dve.engine_nop().then_inc(oh_ok, 1)
            for j, (c, w) in enumerate(SPANS):
                dve.wait_ge(oht_ps, j + 1)
                dve.tensor_copy(OHT[:, c:c + w], ps[0:E_FFN, 5 + j, 0:w]).then_inc(oht_ok, 1)
            dve.wait_ge(mask_ok, 3 * E_FFN)
            for u, (g, j) in enumerate(UP):
                c, w = SPANS[j]
                dve.wait_ge(gelu_ok, u + 1)
                dve.tensor_tensor(HT[:, g, c:c + w], HT[:, g, c:c + w], MASK[:, g // KF, c:c + w], ALU.mult).then_inc(ht_ok, 1)
            for u in range(2 * T):
                s, t = divmod(u, T)
                part = X1[:, t, 384 * s:384 * s + 384]
                dve.wait_ge(down_ok, u + 1)
                dve.tensor_tensor(part, ps[0:R, 4 + u % 4, 0:384], part, ALU.add).then_inc(out_ok, 1)

        @block.tensor
        def _(pe):
            for t in range(T):
                pe.wait_ge(xn_ok, t + 1)
                for j in range(2):
                    if t >= 2:
                        pe.wait_ge(x2_ok, 2 * (t - 2) + j + 1)
                    for k in range(3):
                        tr = pe.transpose(ps[:, 2 * (t % 2) + j, R * k:R * k + R],
                                          XN[t % 2][:, (3 * j + k) * 128:(3 * j + k + 1) * 128], m.ident[0:R, 0:R])
                    tr.then_inc(xt_ok, 1)
            pe.wait_ge(row_in, 16 * 9)
            for t in range(T):
                pe.wait_ge(x2_ok, 2 * t + 2)
                for k in range(KD):
                    mm = pe.matmul(ps[0:R, 4, E_FFN * t:E_FFN * (t + 1)], X2T[:, k, R * t:R * t + R], GW[:, k, :],
                                   start=k == 0, stop=k == KD - 1)
            mm.then_inc(gate_ok, 1)
            pe.wait_ge(oh_ok, 1)
            for j, (c, w) in enumerate(SPANS):
                for i in range(w // R):
                    tr = pe.transpose(ps[0:E_FFN, 5 + j, R * i:R * i + R], OH[:, c // R + i, :], m.ident[0:R, 0:R])
                tr.then_inc(oht_ps, 1)
            pe.wait_ge(oht_ok, 3)
            pe.wait_ge(sel_ok, E_FFN)
            for i in range(3 * E_FFN):
                e, (c, w) = i // 3, SPANS[i % 3]
                if i >= 2:
                    pe.wait_ge(mask_ok, i - 1)
                pe.matmul(ps[:, i % 2, 0:w], SEL[:, e, :], OHT[:, c:c + w], start=True, stop=True).then_inc(mask_ps, 1)
            for u, (g, j) in enumerate(UP):
                e, f, (c, w) = g // KF, g % KF, SPANS[j]
                pe.wait_ge(w1_in[e % 2], 16 * (e // 2 + 1))
                if u >= 2:
                    pe.wait_ge(gelu_ok, u - 1)
                for k in range(KD):
                    mm = pe.matmul(ps[:, 2 + u % 2, 0:w], W1S[e % 2][:, k, 128 * f:128 * f + 128], X2T[:, k, c:c + w],
                                   start=k == 0, stop=k == KD - 1)
                mm.then_inc(up_ok, 1)
            pe.wait_ge(ht_ok, len(UP))
            pe.wait_ge(w2_in, 16 * E_FFN)
            for u in range(2 * T):
                s, t = divmod(u, T)
                if u >= 4:
                    pe.wait_ge(out_ok, u - 3)
                for g in range(G):
                    pe.matmul(ps[0:R, 4 + u % 4, 0:384], HT[:, g, R * t:R * t + R], W2F[:, g, 384 * s:384 * s + 384],
                              start=g == 0, stop=False)
                pe.matmul(ps[0:R, 4 + u % 4, 0:384], OHT[:, R * t:R * t + R], B2F[:, 384 * s:384 * s + 384],
                          start=False, stop=True).then_inc(down_ok, 1)


def gps_block(nc, args, out):
    ctx = ExitStack()
    with ctx:
        def sem(name):
            return ctx.enter_context(nc.semaphore(name))

        def sb(name, shape):
            return ctx.enter_context(nc.sbuf_tensor(name, shape, F32))

        m = Shared()
        m.sem, m.sems = sem, lambda name, n: [sem(f"{name}{i}") for i in range(n)]
        m.arena = sb("arena", [128, 205 * KB])
        m.ident, m.ones, m.eps = sb("ident", [128, 128]), sb("ones", [128, 128]), sb("eps", [128, 1])
        m.stats, m.wstats = sb("stats", [128, 2, 12]), sb("wstats", [128, 2, 12])
        m.mv, m.sd, m.rstd = sb("mv", [128, T, 2]), sb("sd", [128, T]), sb("rstd", [128, T])
        m.mw, m.sw, m.rw = sb("mw", [128, T, 2]), sb("sw", [128, T]), sb("rw", [128, T])
        m.AS, m.AD, m.AS2, m.AS8 = (sb(s, [R, HEADS, T]) for s in ("scores_src", "scores_dst", "src_02", "src_08"))
        m.ps = ctx.enter_context(nc.psum_tensor("ps", [128, 8, 512], F32))
        m.XNT = area(m, 90, KD * N).rearrange("p (k n) -> p k n", k=KD)
        m.C = area(m, 0, T * N // 2, R).bitcast(U16).rearrange("p (t n) -> p t n", t=T)
        m.MT = area(m, 24.5, T * N // 2, R).bitcast(BF16).rearrange("p (t n) -> p t n", t=T)
        m.res_d = nc.dram_tensor("res_scratch", (N, D), F32, kind="Internal").ap()
        m.r1_d = nc.dram_tensor("r1_scratch", (N, HC), F32, kind="Internal").ap()
        m.r2_d = nc.dram_tensor("r2_scratch", (N, D), F32, kind="Internal").ap()
        io = Shared()
        io.x, io.src, io.dst = args["x"], args["src"], args["dst"]
        io.W1, io.a_src1, io.a_dst1 = args["L0_gnn_W1"], args["L0_gnn_a_src1"], args["L0_gnn_a_dst1"]
        io.b1, io.g1, io.be1 = args["L0_gnn_b1"], args["L0_gnn_g1"], args["L0_gnn_be1"]
        io.Wr1, io.br1, io.W2 = args["L0_gnn_Wr1"], args["L0_gnn_br1"], args["L0_gnn_W2"]
        io.a_src2, io.a_dst2, io.b2 = args["L0_gnn_a_src2"], args["L0_gnn_a_dst2"], args["L0_gnn_b2"]
        io.g2, io.be2, io.Wr2 = args["L0_gnn_g2"], args["L0_gnn_be2"], args["L0_gnn_Wr2"]
        io.br2, io.W_qkv, io.b_qkv = args["L0_gnn_br2"], args["L0_mix_W_qkv"], args["L0_mix_b_qkv"]
        io.W_out, io.b_out, io.gate_w = args["L0_mix_W_out"], args["L0_mix_b_out"], args["L0_ffn_gate_w"]
        io.gate_b, io.gate_center, io.w1 = args["L0_ffn_gate_b"], args["L0_ffn_gate_center"], args["L0_ffn_w1"]
        io.fb1, io.w2, io.fb2 = args["L0_ffn_b1"], args["L0_ffn_w2"], args["L0_ffn_b2"]
        io.out = out
        mixer_phase(nc, m, io)
        graph_phase(nc, m, io)
        gat1_phase(nc, m, io)
        gat2_phase(nc, m, io)
        ffn_phase(nc, m, io)


def kernel(**inputs):
    import numpy as _np
    import concourse.bacc as _bacc
    from concourse import mybir as _mybir
    from concourse.bass_utils import run_bass_kernel_spmd as _run

    nc = _bacc.Bacc("TRN2", target_bir_lowering=False, num_devices=1)
    arrays, args = {}, {}
    for name in inputs:
        a = _np.ascontiguousarray(inputs[name])
        arrays[f"in_{name}_dram"] = a
        args[name] = nc.dram_tensor(f"in_{name}_dram", a.shape, _mybir.dt.from_np(a.dtype), kind="ExternalInput").ap()
    out = nc.dram_tensor("out_0_dram", (N, D), F32, kind="ExternalOutput").ap()
    gps_block(nc, args, out)
    r = _run(nc, [arrays], core_ids=[0])
    return r.results[0]["out_0_dram"]
```
